# Optimizing a Trainium2 kernel written in Bass

```python
import numpy as np
import jax
import jax.numpy as jnp

def _softmax(x, axis=-1):
    return jax.nn.softmax(x, axis=axis)

def _gelu(x):
    return jax.nn.gelu(x, approximate=True)

def _silu(x):
    return jax.nn.silu(x)

def _sigmoid(x):
    return jax.nn.sigmoid(x)

def _layernorm(x, axis=-1, eps=1e-05):
    m = jnp.mean(x, axis=axis, keepdims=True)
    v = jnp.var(x, axis=axis, keepdims=True)
    return (x - m) / jnp.sqrt(v + eps)

def _scatter_add(tgt, idx, src, axis=0):
    return tgt.at[idx].add(src)

def _segment_sum(src, seg, n):
    return jax.ops.segment_sum(src, seg, n)
kernel_name = 'mk_cond_resid_d2_seqx_r4_b7c9f4'

def setup_inputs(seed: int=0):
    np.random.seed(seed)
    _w = jnp.asarray

    def _rec_inputs():
        import jax
        import jax.numpy as jnp
        _rk = jax.random.key(seed)
        x = -0.000125 + 0.9999 * jax.random.normal(jax.random.fold_in(_rk, 1), (32, 256, 256), jnp.float32)
        _lenS = 256 - jax.random.randint(jax.random.fold_in(_rk, 7), (32,), 0, max(1, 256 // 4) + 1, jnp.int32)
        _lenS2 = 256 - jax.random.randint(jax.random.fold_in(_rk, 8), (32,), 0, max(1, 256 // 4) + 1, jnp.int32)
        cond_1024 = 0.00782532 + 1.00527 * jax.random.normal(jax.random.fold_in(_rk, 11), (32, 256), jnp.float32)
        return (x, cond_1024)
    x, cond_1024 = _rec_inputs()

    def _L0_cond_setup():
        import jax, jax.numpy as jnp
        import numpy as np
        INV_SQRT2 = 0.7071067811865476
        key = jax.random.key(seed)
        k1, k2, k3, k4 = jax.random.split(key, 4)
        B, N, d = (8, 1024, 256)
        scale = 1.0 / np.sqrt(d)
        return {'v': jax.random.normal(k1, (B, N, d), dtype=jnp.float32), 'q_pool': jax.random.normal(k2, (B, d), dtype=jnp.float32), 'W1': jax.random.normal(k3, (d, d), dtype=jnp.float32) * scale, 'b1': jnp.zeros((d,), dtype=jnp.float32), 'W2': jax.random.normal(k4, (d, d), dtype=jnp.float32) * scale, 'b2': jnp.zeros((d,), dtype=jnp.float32)}
    _L0_cond_all = _L0_cond_setup()
    _L0_cond_in = {k: v for k, v in _L0_cond_all.items() if k in ('W1', 'b1', 'W2', 'b2')}
    del _L0_cond_all

    def _L1_cond_setup():
        import jax, jax.numpy as jnp
        import numpy as np
        N, T, D, H = (64, 128, 256, 256)
        key = jax.random.key(seed)
        k1, k2, k3, k4 = jax.random.split(key, 4)
        x = jax.random.normal(k1, (N, T, D), dtype=jnp.float32)
        h0 = jax.random.normal(k2, (N, H), dtype=jnp.float32)
        Wx = jax.random.normal(k3, (D, H), dtype=jnp.float32) / np.sqrt(D)
        Wh = jax.random.normal(k4, (H, H), dtype=jnp.float32) / np.sqrt(H)
        b = jnp.zeros((H,), dtype=jnp.float32)
        return {'x': x, 'h0': h0, 'Wx': Wx, 'Wh': Wh, 'b': b}
    _L1_cond_all = _L1_cond_setup()
    _L1_cond_in = {k: v for k, v in _L1_cond_all.items() if k in ('Wx', 'Wh', 'b')}
    del _L1_cond_all
    return {'x': x, 'cond_1024': cond_1024, 'L0_cond_W1': _L0_cond_in['W1'], 'L0_cond_b1': _L0_cond_in['b1'], 'L0_cond_W2': _L0_cond_in['W2'], 'L0_cond_b2': _L0_cond_in['b2'], 'L1_cond_Wx': _L1_cond_in['Wx'], 'L1_cond_Wh': _L1_cond_in['Wh'], 'L1_cond_b': _L1_cond_in['b']}

def reference(x, cond_1024, L0_cond_W1, L0_cond_b1, L0_cond_W2, L0_cond_b2, L1_cond_Wx, L1_cond_Wh, L1_cond_b):
    import jax
    import jax.numpy as jnp

    def _L0_cond_ref(v, q_pool, W1, b1, W2, b2):
        import jax, jax.numpy as jnp
        import numpy as np
        INV_SQRT2 = 0.7071067811865476
        B, N, d = v.shape
        h = jax.nn.silu(q_pool @ W1.T + b1)
        gate = jax.nn.sigmoid(h @ W2.T + b2)[:, None, :]
        levels = int(np.log2(N))
        a = v
        details = []
        for _ in range(levels):
            e, o = (a[:, 0::2], a[:, 1::2])
            details.append((e - o) * INV_SQRT2)
            a = (e + o) * INV_SQRT2
        a = a * gate
        for dc in reversed(details):
            dc = dc * gate
            e = (a + dc) * INV_SQRT2
            o = (a - dc) * INV_SQRT2
            n = e.shape[1]
            a = jnp.stack([e, o], axis=2).reshape(B, 2 * n, d)
        return v + a

    def _L1_cond_ref(x, h0, Wx, Wh, b):
        import jax, jax.numpy as jnp
        import numpy as np
        N, T, D, H = (64, 128, 256, 256)
        xW = jnp.einsum('ntd,dh->nth', x, Wx) + b
        xW_t = jnp.swapaxes(xW, 0, 1)

        def step(prev_h, xw):
            next_h = jnp.tanh(prev_h @ Wh + xw)
            return (next_h, next_h)
        _, h_t = jax.lax.scan(step, h0, xW_t)
        return jnp.swapaxes(h_t, 0, 1)
    x = x + _L0_cond_ref(x, cond_1024, L0_cond_W1, L0_cond_b1, L0_cond_W2, L0_cond_b2)
    x = x + _L1_cond_ref(x, cond_1024, L1_cond_Wx, L1_cond_Wh, L1_cond_b)
    return x

_drawn_inputs = setup_inputs


def setup_inputs(seed=0):
    import zlib

    import numpy as np

    out = dict(_drawn_inputs(seed))
    spreads = {'L0_cond_b1': (0.0, 0.8), 'L0_cond_b2': (0.0, 0.8), 'L1_cond_b': (0.0, 0.475)}
    factors = {}
    for name, (base, spread) in spreads.items():
        noise = np.random.default_rng([zlib.crc32(name.encode()), seed]).standard_normal(out[name].shape)
        drawn = base * np.exp(spread * noise) if base else spread * noise
        out[name] = jnp.asarray(drawn.astype(out[name].dtype))
    for name, factor in factors.items():
        out[name] = (out[name] * factor).astype(out[name].dtype)
    return out
```

```python
from contextlib import ExitStack

import concourse.bass as bass
from concourse import mybir

F32 = mybir.dt.float32
BF16 = mybir.dt.bfloat16
ALU = mybir.AluOpType
ACT = mybir.ActivationFunctionType

P = 128
DMA = 16


def build(nc, x, cond, w1, b1, w2, b2, wx, wh, b, out):
    B, T, D = x.shape
    HALVES = D // P
    TS = P // B
    CT = 512 // P
    CS = CT * TS
    PS = 2 * CS
    PT = 2 * CT
    PAIRS = T // PS
    CHUNKS = T // CS
    LOAD = DMA * TS
    assert (B, D, HALVES) == (32, 256, 2) and T % PS == 0 and PAIRS >= 3

    x_view = x.rearrange("b (c t q) d -> c q b t d", t=CT, q=TS)
    out_view = out.rearrange("b (c t q) d -> c q b t d", t=CT, q=TS)

    with ExitStack() as ctx:
        def sb(name, shape, dt=F32):
            return ctx.enter_context(nc.sbuf_tensor(name, shape, dt))

        def sem(name):
            return ctx.enter_context(nc.semaphore(name))

        w1_sb = sb("w1_sb", [P, HALVES, D])
        w2_sb = sb("w2_sb", [P, HALVES, D])
        wx_sb = sb("wx_sb", [P, HALVES, D])
        wh_sb = sb("wh_sb", [P, HALVES, D])
        cond_sb = sb("cond_sb", [B, D])
        gate_bias_rows = sb("gate_bias_rows", [B, P])
        b_rows = sb("b_rows", [P, D])
        identity = sb("identity", [P, P])
        ones = sb("ones", [P, 512], BF16)

        w1_t = sb("w1_t", [P, HALVES, D])
        w2_t = sb("w2_t", [P, HALVES, D])
        q_t = sb("q_t", [P, HALVES, B])
        gate_bias = sb("gate_bias", [P, 2 * HALVES])
        z = sb("z", [P, HALVES, B])
        tanh_z = sb("tanh_z", [P, HALVES, B])
        silu2 = sb("silu2", [P, HALVES, B])
        g_t = sb("g_t", [P, HALVES, B])
        g_t_tile = sb("g_t_tile", [P, HALVES, TS, B])
        g_rows = sb("g_rows", [P, D])

        b_hi = sb("b_hi", [P, D], BF16)
        b_rest = sb("b_rest", [P, D])
        b_mid = sb("b_mid", [P, D], BF16)
        b_last = sb("b_last", [P, D])
        b_split = sb("b_split", [P, D], BF16)

        x_raw = sb("x_raw", [P, 2, CT, D])
        x1_rows = sb("x1_rows", [P, T // TS, D])
        x1_t = sb("x1_t", [P, HALVES, 2, CS * B])
        h_t = sb("h_t", [P, HALVES, PS, B])
        out_rows = sb("out_rows", [P, 2, CT, D])

        pre = [[ctx.enter_context(nc.psum_tensor(f"pre_{m}{s}", [P, CS * B], F32)) for s in range(2)]
               for m in range(HALVES)]
        x_t_ps = [ctx.enter_context(nc.psum_tensor(f"x_t_ps_{k}", [P, CT * P], F32)) for k in range(HALVES)]
        h_rows_ps = [ctx.enter_context(nc.psum_tensor(f"h_rows_ps_{s}", [P, 512], F32)) for s in range(2)]
        w1_t_ps, w2_t_ps = pre[0][1], pre[1][1]
        z1_ps = h_rows_ps[0][:, 0:HALVES * B]
        z2_ps = h_rows_ps[0][:, HALVES * B:2 * HALVES * B]
        q_t_ps = h_rows_ps[1][:, 0:HALVES * B]
        gate_bias_ps = h_rows_ps[1][:, HALVES * B:HALVES * B + B]
        g_rows_ps = h_rows_ps[1][:, 0:D]

        cond_loaded = sem("cond_loaded")
        gate_bias_zeroed = sem("gate_bias_zeroed")
        w1_loaded = sem("w1_loaded")
        w2_loaded = sem("w2_loaded")
        wx_loaded = sem("wx_loaded")
        wh_loaded = sem("wh_loaded")
        b_zeroed = sem("b_zeroed")
        b_loaded = sem("b_loaded")
        identity_zeroed = sem("identity_zeroed")
        identity_ready = sem("identity_ready")
        ones_ready = sem("ones_ready")
        q_transposed = sem("q_transposed")
        q_ready = sem("q_ready")
        w1_transposed = sem("w1_transposed")
        w1_t_ready = sem("w1_t_ready")
        w2_transposed = sem("w2_transposed")
        w2_t_ready = sem("w2_t_ready")
        z1_product = sem("z1_product")
        z2_product = sem("z2_product")
        z_ready = sem("z_ready")
        tanh_z_ready = sem("tanh_z_ready")
        silu_ready = sem("silu_ready")
        g_t_ready = sem("g_t_ready")
        g_tile_ready = sem("g_tile_ready")
        g_transposed = sem("g_transposed")
        g_rows_ready = sem("g_rows_ready")
        b_step = sem("b_step")
        b_split_ready = sem("b_split_ready")

        x_loaded = [sem(f"x_loaded_{s}") for s in range(2)]
        x_transposed = sem("x_transposed")
        x1_t_ready = sem("x1_t_ready")
        x1_rows_ready = sem("x1_rows_ready")
        inputs_laid = sem("inputs_laid")
        pre_ready = [sem(f"pre_ready_{m}") for m in range(HALVES)]
        h_ready = [sem(f"h_ready_{m}") for m in range(HALVES)]
        h_rows_ready = sem("h_rows_ready")
        out_ready = sem("out_ready")
        out_stored = [sem(f"out_stored_{s}") for s in range(2)]

        block = ctx.enter_context(nc.Block())

        @block.sync
        def _(sp):
            def load(c, slot):
                for q in range(TS):
                    sp.dma_start(x_raw[q * B:(q + 1) * B, slot, :, :], x_view[c, q]).then_inc(x_loaded[slot], DMA)

            def store(c, slot):
                for q in range(TS):
                    sp.dma_start(out_view[c, q], out_rows[q * B:(q + 1) * B, slot, :, :])\
                        .then_inc(out_stored[slot], DMA)

            def turn(i, first=False, before_last=False, last=False):
                for s in range(2):
                    c = 2 * i + s
                    if not last and not (s == 1 and before_last):
                        sp.wait_ge(x_transposed, HALVES * (c + 2))
                        sp.wait_ge(x1_rows_ready, c + 2)
                        load(c + 3, 1 - s)
                    if not (first and s == 0):
                        sp.wait_ge(out_ready, CT * c)
                        store(c - 1, 1 - s)

            load(0, 0)
            load(1, 1)
            sp.wait_ge(x_transposed, HALVES)
            sp.wait_ge(x1_rows_ready, 1)
            load(2, 0)
            turn(0, first=True)
            with sp.Fori(1, PAIRS - 2) as i:
                turn(i)
            turn(PAIRS - 2, before_last=True)
            turn(PAIRS - 1, last=True)
            sp.wait_ge(out_ready, CT * CHUNKS)
            store(CHUNKS - 1, 1)
            for s in range(2):
                sp.wait_ge(out_stored[s], LOAD * (CHUNKS // 2))

        @block.gpsimd
        def _(pool):
            nc.gpsimd.memset(identity[:], 0.0).then_inc(identity_zeroed, 1)
            nc.gpsimd.memset(gate_bias_rows[:], 0.0).then_inc(gate_bias_zeroed, 1)
            nc.gpsimd.memset(b_rows[:], 0.0).then_inc(b_zeroed, 1)
            pool.wait_ge(identity_zeroed, 1)
            nc.gpsimd.affine_select(out=identity[:], in_=identity[:], compare_op=ALU.not_equal, fill=1.0, base=0,
                                    pattern=[[-1, P]], channel_multiplier=1).then_inc(identity_ready, 1)
            nc.gpsimd.memset(ones[:], 1.0).then_inc(ones_ready, 1)

        @block.scalar
        def _(act):
            act.dma_start(cond_sb[:], cond).then_inc(cond_loaded, DMA)
            act.dma_start(w1_sb[:], w1.rearrange("(k p) n -> p k n", p=P)).then_inc(w1_loaded, DMA)
            act.wait_ge(gate_bias_zeroed, 1)
            act.dma_start(gate_bias_rows[0:HALVES, :], b1.rearrange("(k p) -> k p", p=P)).then_inc(cond_loaded, DMA)
            act.dma_start(gate_bias_rows[HALVES:2 * HALVES, :], b2.rearrange("(k p) -> k p", p=P))\
               .then_inc(cond_loaded, DMA)
            act.dma_start(w2_sb[:], w2.rearrange("(k p) n -> p k n", p=P)).then_inc(w2_loaded, DMA)
            act.dma_start(wx_sb[:], wx.rearrange("(k p) n -> p k n", p=P)).then_inc(wx_loaded, DMA)
            act.wait_ge(b_zeroed, 1)
            for r in range(3):
                act.dma_start(b_rows[32 * r:32 * r + 1, :], b.rearrange("(a n) -> a n", a=1)).then_inc(b_loaded, DMA)
            act.dma_start(wh_sb[:], wh.rearrange("(k p) n -> p k n", p=P)).then_inc(wh_loaded, DMA)
            for layer in range(2):
                act.wait_ge(z_ready, layer + 1)
                nc.scalar.activation(tanh_z[:], z[:], ACT.Tanh, scale=0.5).then_inc(tanh_z_ready, 1)

            def step(t, s):
                slot, r = s // CS, s % CS
                for m in range(HALVES):
                    act.wait_ge(pre_ready[m], t + 1)
                    nc.scalar.activation(h_t[:, m, s, :], pre[m][slot][:, r * B:(r + 1) * B], ACT.Tanh)\
                        .then_inc(h_ready[m], 1)

            with act.Fori(0, PAIRS) as i:
                for s in range(PS):
                    step(PS * i + s, s)

        @block.tensor
        def _(pe):
            def transpose_x(slot, n):
                k, tile = n // CT, n % CT
                done = nc.tensor.transpose(x_t_ps[k][:, tile * P:(tile + 1) * P],
                                           x_raw[:, slot, tile, k * P:(k + 1) * P], identity[:])
                if tile == CT - 1:
                    done.then_inc(x_transposed, 1)

            def lay_bias(slot, m):
                nc.tensor.matmul(pre[m][slot][:], b_split[:, m * P:(m + 1) * P], ones[:],
                                 start=True, stop=False, skip_group_check=True)

            def lay_input(slot, n):
                k, m, tile = n // (2 * CT), n // CT % 2, n % CT
                cols = slice(tile * P, (tile + 1) * P)
                done = nc.tensor.matmul(pre[m][slot][:, cols], wx_sb[:, k, m * P:(m + 1) * P], x1_t[:, k, slot, cols],
                                        start=False, stop=False, skip_group_check=True)
                if n == 4 * CT - 1:
                    done.then_inc(inputs_laid, 1)

            def recur(s, k, m):
                slot, r = s // CS, s % CS
                return nc.tensor.matmul(pre[m][slot][:, r * B:(r + 1) * B], wh_sb[:, k, m * P:(m + 1) * P],
                                        h_t[:, k, (s - 1) % PS, :], start=False, stop=(k == 1), skip_group_check=True)

            def transpose_h(tile, half):
                done = nc.tensor.transpose(h_rows_ps[tile % 2][:, half * P:(half + 1) * P],
                                           h_t[:, half, tile * TS:(tile + 1) * TS, :].rearrange("p s b -> p (s b)"),
                                           identity[:])
                if half == HALVES - 1:
                    done.then_inc(h_rows_ready, 1)

            pe.wait_ge(identity_ready, 1)
            pe.wait_ge(cond_loaded, 3 * DMA)
            for k in range(HALVES):
                nc.tensor.transpose(q_t_ps[:, k * B:(k + 1) * B], cond_sb[:, k * P:(k + 1) * P], identity[0:B, 0:B])
            nc.tensor.transpose(gate_bias_ps, gate_bias_rows[:], identity[0:B, 0:B]).then_inc(q_transposed, 1)
            pe.wait_ge(w1_loaded, DMA)
            for k in range(HALVES):
                for m in range(HALVES):
                    done = nc.tensor.transpose(w1_t_ps[:, k * D + m * P:k * D + (m + 1) * P],
                                               w1_sb[:, m, k * P:(k + 1) * P], identity[:])
            done.then_inc(w1_transposed, 1)
            pe.wait_ge(w2_loaded, DMA)
            for k in range(HALVES):
                for m in range(HALVES):
                    done = nc.tensor.transpose(w2_t_ps[:, k * D + m * P:k * D + (m + 1) * P],
                                               w2_sb[:, m, k * P:(k + 1) * P], identity[:])
            done.then_inc(w2_transposed, 1)
            pe.wait_ge(x_loaded[0], LOAD)
            for n in range(HALVES * CT):
                transpose_x(0, n)
            pe.wait_ge(q_ready, 1)
            pe.wait_ge(w1_t_ready, 1)
            for m in range(HALVES):
                for k in range(HALVES):
                    done = nc.tensor.matmul(z1_ps[:, m * B:(m + 1) * B], w1_t[:, k, m * P:(m + 1) * P], q_t[:, k, :],
                                            start=(k == 0), stop=(k == HALVES - 1))
            done.then_inc(z1_product, 1)
            pe.wait_ge(silu_ready, 1)
            pe.wait_ge(w2_t_ready, 1)
            for m in range(HALVES):
                for k in range(HALVES):
                    done = nc.tensor.matmul(z2_ps[:, m * B:(m + 1) * B], w2_t[:, k, m * P:(m + 1) * P], silu2[:, k, :],
                                            start=(k == 0), stop=(k == HALVES - 1))
            done.then_inc(z2_product, 1)
            pe.wait_ge(g_tile_ready, 1)
            for k in range(HALVES):
                done = nc.tensor.transpose(g_rows_ps[:, k * P:(k + 1) * P],
                                           g_t_tile[:, k, :, :].rearrange("p s b -> p (s b)"), identity[:])
            done.then_inc(g_transposed, 1)
            pe.wait_ge(ones_ready, 1)
            pe.wait_ge(b_split_ready, 3)
            pe.wait_ge(wx_loaded, DMA)
            for m in range(HALVES):
                lay_bias(0, m)
            for k in range(HALVES):
                pe.wait_ge(x1_t_ready, k + 1)
                for n in range(2 * CT):
                    lay_input(0, k * 2 * CT + n)
            pe.wait_ge(x_loaded[1], LOAD)
            for n in range(HALVES * CT):
                transpose_x(1, n)
            pe.wait_ge(wh_loaded, DMA)
            pe.wait_ge(q_ready, 3)

            def fill(i, s, first, last):
                c, slot, r = 2 * i + s // CS, s // CS, s % CS
                group, phase = r // TS, r % TS
                if not (last and slot == 1):
                    if r == 0:
                        pe.wait_ge(x1_t_ready, HALVES * (c + 1) + 1)
                        lay_bias(1 - slot, 0)
                        lay_bias(1 - slot, 1)
                    if r == 2 * CT:
                        pe.wait_ge(x1_t_ready, HALVES * (c + 1) + 2)
                    lay_input(1 - slot, r)
                if phase in (0, TS - 1) and not last:
                    if r == 0:
                        pe.wait_ge(x_loaded[slot], LOAD * (i + 2))
                    transpose_x(slot, 2 * group + phase // (TS - 1))
                if phase in (1, 2) and not (first and slot == 0 and group == 0):
                    tile = (CT * slot + group - 1) % PT
                    if phase == 1 and not (first and CT * slot + group - 1 < 2):
                        pe.wait_ge(out_ready, CT * c + group - 2)
                    transpose_h(tile, phase - 1)

            def turn(i, first=False, last=False):
                for s in range(PS):
                    t = PS * i + s
                    if not (first and s == 0):
                        pe.wait_ge(h_ready[0], t)
                    recur(s, 0, 0)
                    if not (first and s == 0):
                        pe.wait_ge(h_ready[1], t)
                    recur(s, 1, 0).then_inc(pre_ready[0], 1)
                    recur(s, 0, 1)
                    recur(s, 1, 1).then_inc(pre_ready[1], 1)
                    fill(i, s, first, last)

            turn(0, first=True)
            with pe.Fori(1, PAIRS - 1) as i:
                turn(i)
            turn(PAIRS - 1, last=True)
            for m in range(HALVES):
                pe.wait_ge(h_ready[m], T)
            pe.wait_ge(out_ready, T // TS - 2)
            for m in range(HALVES):
                transpose_h(PT - 1, m)

        @block.vector
        def _(dve):
            def scale_rows(c, slot, load_count):
                dve.wait_ge(x_loaded[slot], load_count)
                nc.vector.tensor_tensor(x1_rows[:, bass.ds(CT * c, CT), :], x_raw[:, slot, :, :],
                                        g_rows[:].unsqueeze(1).to_broadcast([P, CT, D]), ALU.mult)\
                    .then_inc(x1_rows_ready, 1)

            def scale_transposed(c, slot, k):
                dve.wait_ge(x_transposed, HALVES * c + k + 1)
                nc.vector.tensor_tensor(x1_t[:, k, slot, :].rearrange("p (s b) -> p s b", b=B),
                                        x_t_ps[k][:].rearrange("p (s b) -> p s b", b=B),
                                        g_t[:, k, :].unsqueeze(1).to_broadcast([P, CS, B]), ALU.mult)\
                    .then_inc(x1_t_ready, 1)

            def add_rows(j, slot, tile):
                dve.wait_ge(h_rows_ready, j + 1)
                nc.vector.tensor_tensor(out_rows[:, slot, tile, :], h_rows_ps[tile % 2][:, 0:D],
                                        x1_rows[:, bass.ds(j, 1), :].rearrange("p a d -> p (a d)"), ALU.add)\
                    .then_inc(out_ready, 1)

            dve.wait_ge(q_transposed, 1)
            nc.vector.tensor_copy(q_t[:].rearrange("p k b -> p (k b)"), q_t_ps).then_inc(q_ready, 1)
            nc.vector.tensor_copy(gate_bias[:], gate_bias_ps[:, 0:2 * HALVES]).then_inc(q_ready, 1)
            dve.wait_ge(w1_transposed, 1)
            nc.vector.tensor_copy(w1_t[:].rearrange("p k n -> p (k n)"), w1_t_ps[:]).then_inc(w1_t_ready, 1)
            dve.wait_ge(w2_transposed, 1)
            nc.vector.tensor_copy(w2_t[:].rearrange("p k n -> p (k n)"), w2_t_ps[:]).then_inc(w2_t_ready, 1)
            dve.wait_ge(q_ready, 2)
            nc.vector.tensor_copy(h_t[:, :, PS - 1, :], q_t[:]).then_inc(q_ready, 1)
            dve.wait_ge(b_loaded, 3 * DMA)
            nc.vector.tensor_copy(b_hi[:], b_rows[:]).then_inc(b_step, 1)
            nc.vector.memset(b_split[:], 0.0).then_inc(b_step, 1)
            dve.wait_ge(b_step, 2)
            nc.vector.tensor_tensor(b_rest[:], b_rows[:], b_hi[:], ALU.subtract).then_inc(b_step, 1)
            dve.wait_ge(b_step, 3)
            nc.vector.tensor_copy(b_mid[:], b_rest[:]).then_inc(b_step, 1)
            dve.wait_ge(b_step, 4)
            nc.vector.tensor_tensor(b_last[:], b_rest[:], b_mid[:], ALU.subtract).then_inc(b_step, 1)
            dve.wait_ge(b_step, 5)
            nc.vector.tensor_copy(b_split[0:32, :], b_hi[0:32, :]).then_inc(b_split_ready, 1)
            nc.vector.tensor_copy(b_split[32:64, :], b_mid[32:64, :]).then_inc(b_split_ready, 1)
            nc.vector.tensor_copy(b_split[64:96, :], b_last[64:96, :]).then_inc(b_split_ready, 1)
            for layer, (z_product, z_ps, half) in enumerate(((z1_product, z1_ps, 1.0), (z2_product, z2_ps, 0.5))):
                dve.wait_ge(z_product, 1)
                for m in range(HALVES):
                    done = nc.vector.tensor_scalar(z[:, m, :], z_ps[:, m * B:(m + 1) * B], half,
                                                   gate_bias[:, layer * HALVES + m:layer * HALVES + m + 1],
                                                   ALU.mult, ALU.add)
                done.then_inc(z_ready, 1)
                dve.wait_ge(tanh_z_ready, layer + 1)
                if layer == 0:
                    nc.vector.scalar_tensor_tensor(out=silu2[:], in0=tanh_z[:], scalar=1.0, in1=z[:],
                                                   op0=ALU.add, op1=ALU.mult).then_inc(silu_ready, 1)
            nc.vector.tensor_scalar(g_t[:], tanh_z[:], 0.5, 2.5, ALU.mult, ALU.add).then_inc(g_t_ready, 1)
            dve.wait_ge(g_t_ready, 1)
            for k in range(HALVES):
                done = nc.vector.tensor_copy(g_t_tile[:, k, :, :], g_t[:, k, :].unsqueeze(1).to_broadcast([P, TS, B]))
            done.then_inc(g_tile_ready, 1)
            for k in range(HALVES):
                scale_transposed(0, 0, k)
            dve.wait_ge(g_transposed, 1)
            nc.vector.tensor_copy(g_rows[:], g_rows_ps).then_inc(g_rows_ready, 1)
            for k in range(HALVES):
                scale_transposed(1, 1, k)
            dve.wait_ge(g_rows_ready, 1)
            scale_rows(0, 0, LOAD)
            scale_rows(1, 1, LOAD)

            def turn(i, first=False, last=False):
                for s in range(2):
                    c = 2 * i + s
                    for group in range(CT):
                        j = CT * c + group - 1
                        tile, slot = (group - 1) % CT, s if group else 1 - s
                        if not (first and s == 0 and group == 0):
                            if tile == 0 and not first:
                                dve.wait_ge(out_stored[slot], LOAD * i)
                            add_rows(j, slot, tile)
                        if not last and group == 0:
                            scale_rows(c + 2, s, LOAD * (i + 2))
                        if not last and group == 2:
                            dve.wait_ge(inputs_laid, c + 1)
                            scale_transposed(c + 2, s, 0)
                    if not last:
                        scale_transposed(c + 2, s, 1)

            turn(0, first=True)
            with dve.Fori(1, PAIRS - 1) as i:
                turn(i)
            turn(PAIRS - 1, last=True)
            add_rows(T // TS - 1, 1, CT - 1)


_INS = ["x", "cond_1024", "L0_cond_W1", "L0_cond_b1", "L0_cond_W2", "L0_cond_b2", "L1_cond_Wx", "L1_cond_Wh",
        "L1_cond_b"]


def kernel(**inputs):
    import numpy as np
    import concourse.bacc as bacc
    from concourse.bass_utils import run_bass_kernel_spmd

    nc = bacc.Bacc("TRN2", target_bir_lowering=False, num_devices=1)
    arrays, args = {}, []
    for name in _INS:
        a = np.ascontiguousarray(inputs[name])
        arrays[f"in_{name}"] = a
        args.append(nc.dram_tensor(f"in_{name}", a.shape, mybir.dt.from_np(a.dtype), kind="ExternalInput").ap())
    args.append(nc.dram_tensor("out_dram", inputs["x"].shape, F32, kind="ExternalOutput").ap())
    build(nc, *args)
    r = run_bass_kernel_spmd(nc, [arrays], core_ids=[0])
    return r.results[0]["out_dram"]
```

```python
from contextlib import ExitStack

import concourse.bass as bass
from concourse import mybir

F32 = mybir.dt.float32
BF16 = mybir.dt.bfloat16
F16 = mybir.dt.float16
ALU = mybir.AluOpType
ACT = mybir.ActivationFunctionType

P = 128
DMA = 16


def build(nc, x, cond, w1, b1, w2, b2, wx, wh, b, out):
    B, T, D = x.shape
    HALVES = D // P
    TS = P // B
    CT = 512 // P
    CS = CT * TS
    PS = 2 * CS
    PT = 2 * CT
    PAIRS = T // PS
    CHUNKS = T // CS
    LOAD = DMA * TS
    assert (B, D, HALVES) == (32, 256, 2) and T % PS == 0 and PAIRS >= 3

    x_view = x.rearrange("b (c t q) d -> c q b t d", t=CT, q=TS)
    out_view = out.rearrange("b (c t q) d -> c q b t d", t=CT, q=TS)

    with ExitStack() as ctx:
        def sb(name, shape, dt=F32):
            return ctx.enter_context(nc.sbuf_tensor(name, shape, dt))

        def sem(name):
            return ctx.enter_context(nc.semaphore(name))

        w1_sb = sb("w1_sb", [P, HALVES, D])
        w2_sb = sb("w2_sb", [P, HALVES, D])
        wx_sb = sb("wx_sb", [P, HALVES, D])
        wh_sb = sb("wh_sb", [P, HALVES, D])
        cond_sb = sb("cond_sb", [B, D])
        gate_bias_rows = sb("gate_bias_rows", [B, P])
        b_rows = sb("b_rows", [P, D])
        identity = sb("identity", [P, P])
        ones = sb("ones", [P, 256], BF16)

        wh_a = sb("wh_a", [P, HALVES, D], BF16)
        wh_b = sb("wh_b", [P, HALVES, D], BF16)
        wh_c = sb("wh_c", [P, HALVES, D], BF16)
        wh_rest = sb("wh_rest", [P, HALVES, D])
        wh_last = sb("wh_last", [P, HALVES, D])

        w1_t = sb("w1_t", [P, HALVES, D])
        w2_t = sb("w2_t", [P, HALVES, D])
        q_t = sb("q_t", [P, HALVES, B])
        gate_bias = sb("gate_bias", [P, 2 * HALVES])
        z = sb("z", [P, HALVES, B])
        tanh_z = sb("tanh_z", [P, HALVES, B])
        silu2 = sb("silu2", [P, HALVES, B])
        g_t = sb("g_t", [P, HALVES, B])
        g_t_tile = sb("g_t_tile", [P, HALVES, TS, B])
        g_rows = sb("g_rows", [P, D])

        b_hi = sb("b_hi", [P, D], BF16)
        b_rest = sb("b_rest", [P, D])
        b_mid = sb("b_mid", [P, D], BF16)
        b_last = sb("b_last", [P, D])
        b_split = sb("b_split", [P, D], BF16)

        x_first = sb("x_first", [P, 2, CT, D])
        x_raw = sb("x_raw", [P, 2, CT, D])
        x1_rows = sb("x1_rows", [P, T // TS, D])
        x1_t = sb("x1_t", [P, HALVES, 2, CS * B])
        h_t = sb("h_t", [P, HALVES, PS, B])
        h1 = sb("h1", [P, 2, HALVES, B], F16)
        h2 = sb("h2", [P, 2, HALVES, B], F16)
        out_rows = sb("out_rows", [P, 2, CT, D])

        pre = [[ctx.enter_context(nc.psum_tensor(f"pre_{s}{e}", [P, CS // 2, HALVES, B], F32)) for e in range(2)]
               for s in range(2)]
        x_t_ps = [ctx.enter_context(nc.psum_tensor(f"x_t_ps_{k}", [P, CT * P], F32)) for k in range(HALVES)]
        h_rows_ps = [ctx.enter_context(nc.psum_tensor(f"h_rows_ps_{s}", [P, 512], F32)) for s in range(2)]
        w1_t_ps, w2_t_ps = [pre[1][e][:].rearrange("p s m b -> p (s m b)") for e in range(2)]
        z1_ps = h_rows_ps[0][:, 0:HALVES * B]
        z2_ps = h_rows_ps[0][:, HALVES * B:2 * HALVES * B]
        q_t_ps = h_rows_ps[1][:, 0:HALVES * B]
        gate_bias_ps = h_rows_ps[1][:, HALVES * B:HALVES * B + B]
        g_rows_ps = h_rows_ps[1][:, 0:D]

        cond_loaded = sem("cond_loaded")
        gate_bias_loaded = sem("gate_bias_loaded")
        gate_bias_zeroed = sem("gate_bias_zeroed")
        w1_loaded = sem("w1_loaded")
        w2_loaded = sem("w2_loaded")
        wx_loaded = sem("wx_loaded")
        wh_loaded = sem("wh_loaded")
        b_zeroed = sem("b_zeroed")
        b_loaded = sem("b_loaded")
        identity_zeroed = sem("identity_zeroed")
        identity_ready = sem("identity_ready")
        ones_ready = sem("ones_ready")
        q_transposed = sem("q_transposed")
        q_ready = sem("q_ready")
        gate_bias_transposed = sem("gate_bias_transposed")
        gate_bias_ready = sem("gate_bias_ready")
        w1_transposed = sem("w1_transposed")
        w1_t_ready = sem("w1_t_ready")
        w2_transposed = sem("w2_transposed")
        w2_t_ready = sem("w2_t_ready")
        z1_product = sem("z1_product")
        z2_product = sem("z2_product")
        z_ready = sem("z_ready")
        tanh_z_ready = sem("tanh_z_ready")
        silu_ready = sem("silu_ready")
        g_t_ready = sem("g_t_ready")
        g_tile_ready = sem("g_tile_ready")
        g_transposed = sem("g_transposed")
        g_rows_ready = sem("g_rows_ready")
        b_step = sem("b_step")
        wh_cast = sem("wh_cast")
        wh_less = sem("wh_less")
        b_split_ready = sem("b_split_ready")

        x_first_loaded = [sem(f"x_first_loaded_{c}") for c in range(2)]
        x_loaded = [sem(f"x_loaded_{s}") for s in range(2)]
        x_transposed = sem("x_transposed")
        x1_t_ready = sem("x1_t_ready")
        x1_rows_ready = sem("x1_rows_ready")
        inputs_laid = sem("inputs_laid")
        pre_ready = sem("pre_ready")
        h1_ready = sem("h1_ready")
        h_ready = [sem(f"h_ready_{m}") for m in range(HALVES)]
        h2_ready = [sem(f"h2_ready_{m}") for m in range(HALVES)]
        h_rows_ready = sem("h_rows_ready")
        out_ready = sem("out_ready")
        out_stored = [sem(f"out_stored_{s}") for s in range(2)]
        out_last_stored = sem("out_last_stored")

        block = ctx.enter_context(nc.Block())

        @block.sync
        def _(sp):
            def load(place, c, slot, loaded):
                for q in range(TS):
                    sp.dma_start(place[q * B:(q + 1) * B, slot, :, :], x_view[c, q]).then_inc(loaded, DMA)

            def store(c, slot):
                for q in range(TS):
                    sp.dma_start(out_view[c, q], out_rows[q * B:(q + 1) * B, slot, :, :])\
                        .then_inc(out_stored[slot], DMA)

            def turn(i, first=False, before_last=False, last=False):
                for s in range(2):
                    c = 2 * i + s
                    if not (first and s == 0) and not (before_last and s == 1) and not last:
                        sp.wait_ge(x_transposed, HALVES * (c + 2))
                        sp.wait_ge(x1_rows_ready, c + 2)
                        load(x_raw, c + 3, 1 - s, x_loaded[1 - s])
                    if not (first and s == 0):
                        sp.wait_ge(out_ready, CT * c)
                        store(c - 1, 1 - s)

            sp.dma_start(cond_sb[:], cond).then_inc(cond_loaded, DMA)
            for c in range(2):
                load(x_first, c, c, x_first_loaded[c])
            for c in range(2):
                load(x_raw, c + 2, c, x_loaded[c])
            turn(0, first=True)
            with sp.Fori(1, PAIRS - 2) as i:
                turn(i)
            turn(PAIRS - 2, before_last=True)
            turn(PAIRS - 1, last=True)
            for tile in range(CT):
                sp.wait_ge(out_ready, CT * (CHUNKS - 1) + tile + 1)
                for q in range(TS):
                    sp.dma_start(out_view[CHUNKS - 1, q, :, tile, :], out_rows[q * B:(q + 1) * B, 1, tile, :])\
                        .then_inc(out_last_stored, DMA)
            sp.wait_ge(out_stored[0], LOAD * (CHUNKS // 2))
            sp.wait_ge(out_stored[1], LOAD * (CHUNKS // 2 - 1))
            sp.wait_ge(out_last_stored, LOAD * CT)

        @block.gpsimd
        def _(pool):
            nc.gpsimd.memset(identity[:], 0.0).then_inc(identity_zeroed, 1)
            nc.gpsimd.memset(gate_bias_rows[:], 0.0).then_inc(gate_bias_zeroed, 1)
            nc.gpsimd.memset(b_rows[:], 0.0).then_inc(b_zeroed, 1)
            pool.dma_start(wh_sb[:], wh.rearrange("(k p) n -> p k n", p=P)).then_inc(wh_loaded, DMA)
            pool.wait_ge(identity_zeroed, 1)
            nc.gpsimd.affine_select(out=identity[:], in_=identity[:], compare_op=ALU.not_equal, fill=1.0, base=0,
                                    pattern=[[-1, P]], channel_multiplier=1).then_inc(identity_ready, 1)
            pool.wait_ge(b_zeroed, 1)
            for r in range(3):
                pool.dma_start(b_rows[32 * r:32 * r + 1, :], b.rearrange("(a n) -> a n", a=1)).then_inc(b_loaded, DMA)
            nc.gpsimd.memset(ones[:], 1.0).then_inc(ones_ready, 1)
            nc.gpsimd.memset(b_split[:], 0.0).then_inc(b_step, 1)
            pool.wait_ge(b_loaded, 3 * DMA)
            nc.gpsimd.tensor_copy(b_hi[:], b_rows[:]).then_inc(b_step, 1)
            pool.wait_ge(b_step, 2)
            nc.gpsimd.tensor_tensor(b_rest[:], b_rows[:], b_hi[:], ALU.subtract).then_inc(b_step, 1)
            pool.wait_ge(b_step, 3)
            nc.gpsimd.tensor_copy(b_mid[:], b_rest[:]).then_inc(b_step, 1)
            pool.wait_ge(b_step, 4)
            nc.gpsimd.tensor_tensor(b_last[:], b_rest[:], b_mid[:], ALU.subtract).then_inc(b_step, 1)
            pool.wait_ge(b_step, 5)
            nc.gpsimd.tensor_copy(b_split[0:32, :], b_hi[0:32, :]).then_inc(b_split_ready, 1)
            nc.gpsimd.tensor_copy(b_split[32:64, :], b_mid[32:64, :]).then_inc(b_split_ready, 1)
            nc.gpsimd.tensor_copy(b_split[64:96, :], b_last[64:96, :]).then_inc(b_split_ready, 1)

        @block.scalar
        def _(act):
            act.dma_start(w1_sb[:], w1.rearrange("(k p) n -> p k n", p=P)).then_inc(w1_loaded, DMA)
            act.dma_start(w2_sb[:], w2.rearrange("(k p) n -> p k n", p=P)).then_inc(w2_loaded, DMA)
            act.wait_ge(gate_bias_zeroed, 1)
            for n, gate_b in enumerate((b1, b2)):
                act.dma_start(gate_bias_rows[n * HALVES:(n + 1) * HALVES, :], gate_b.rearrange("(k p) -> k p", p=P))\
                   .then_inc(gate_bias_loaded, DMA)
            act.dma_start(wx_sb[:], wx.rearrange("(k p) n -> p k n", p=P)).then_inc(wx_loaded, DMA)
            act.wait_ge(wh_loaded, DMA)
            nc.scalar.activation(wh_a[:], wh_sb[:], ACT.Copy).then_inc(wh_cast, 1)
            for layer, (part, rest) in enumerate(((wh_b, wh_rest), (wh_c, wh_last))):
                act.wait_ge(z_ready, layer + 1)
                nc.scalar.activation(tanh_z[:], z[:], ACT.Tanh, scale=0.5).then_inc(tanh_z_ready, 1)
                act.wait_ge(wh_less, layer + 1)
                nc.scalar.activation(part[:], rest[:], ACT.Copy).then_inc(wh_cast, 1)

            def step(t, s):
                z_t = pre[s // CS][s % 2][:, s % CS // 2, :, :]
                act.wait_ge(pre_ready, t + 1)
                nc.scalar.activation(h1[:, s % 2, :, :], z_t, ACT.Tanh).then_inc(h1_ready, 1)
                for m in range(HALVES):
                    nc.scalar.activation(h_t[:, m, s, :], z_t[:, m, :], ACT.Tanh).then_inc(h_ready[m], 1)

            with act.Fori(0, PAIRS) as i:
                for s in range(PS):
                    step(PS * i + s, s)

        @block.tensor
        def _(pe):
            def transpose_x(place, slot, n):
                k, tile = n // CT, n % CT
                done = nc.tensor.transpose(x_t_ps[k][:, tile * P:(tile + 1) * P],
                                           place[:, slot, tile, k * P:(k + 1) * P], identity[:])
                if tile == CT - 1:
                    done.then_inc(x_transposed, 1)

            def lay_bias(slot, n):
                e, m = n // HALVES, n % HALVES
                nc.tensor.matmul(pre[slot][e][:, :, m, :], b_split[:, m * P:(m + 1) * P], ones[:, 0:CS // 2 * B],
                                 start=(m == 0), stop=False, skip_group_check=True)

            def lay_input(slot, k, e, m, part, whole=False):
                steps = slice(part * CS // 4, (part + 1) * CS // 4)
                x1_steps = x1_t[:, k, slot, :].rearrange("p (s e b) -> p s e b", e=2, b=B)[:, steps, e, :]
                done = nc.tensor.matmul(pre[slot][e][:, steps, m, :], wx_sb[:, k, m * P:(m + 1) * P], x1_steps,
                                        start=False, stop=False, skip_group_check=True)
                if whole:
                    done.then_inc(inputs_laid, 1)
                return done

            def lay_nth(slot, n):
                lay_input(slot, n // 8, n // 4 % 2, n // 2 % 2, n % 2, whole=(n == 15))

            def recur(s, k, m, weights, h_part, stop=False):
                return nc.tensor.matmul(pre[s // CS][s % 2][:, s % CS // 2, m, :], weights[:, k, m * P:(m + 1) * P],
                                        h_part, start=False, stop=stop, skip_group_check=True)

            def transpose_h(tile, half):
                done = nc.tensor.transpose(h_rows_ps[tile % 2][:, half * P:(half + 1) * P],
                                           h_t[:, half, tile * TS:(tile + 1) * TS, :].rearrange("p s b -> p (s b)"),
                                           identity[:])
                if half == HALVES - 1:
                    done.then_inc(h_rows_ready, 1)

            def transpose_weights(w_t_ps, w_sb):
                for k in range(HALVES):
                    for m in range(HALVES):
                        done = nc.tensor.transpose(w_t_ps[:, k * D + m * P:k * D + (m + 1) * P],
                                                   w_sb[:, m, k * P:(k + 1) * P], identity[:])
                return done

            def gate_layer(z_ps, w_t, operand):
                for m in range(HALVES):
                    for k in range(HALVES):
                        done = nc.tensor.matmul(z_ps[:, m * B:(m + 1) * B], w_t[:, k, m * P:(m + 1) * P],
                                                operand[:, k, :], start=(k == 0), stop=(k == HALVES - 1))
                return done

            pe.wait_ge(identity_ready, 1)
            pe.wait_ge(cond_loaded, DMA)
            for k in range(HALVES):
                done = nc.tensor.transpose(q_t_ps[:, k * B:(k + 1) * B], cond_sb[:, k * P:(k + 1) * P],
                                           identity[0:B, 0:B])
            done.then_inc(q_transposed, 1)
            pe.wait_ge(w1_loaded, DMA)
            transpose_weights(w1_t_ps, w1_sb).then_inc(w1_transposed, 1)
            pe.wait_ge(w2_loaded, DMA)
            transpose_weights(w2_t_ps, w2_sb).then_inc(w2_transposed, 1)
            pe.wait_ge(gate_bias_loaded, 2 * DMA)
            pe.wait_ge(q_ready, 1)
            nc.tensor.transpose(gate_bias_ps, gate_bias_rows[:], identity[0:B, 0:B]).then_inc(gate_bias_transposed, 1)
            pe.wait_ge(w1_t_ready, 1)
            gate_layer(z1_ps, w1_t, q_t).then_inc(z1_product, 1)
            pe.wait_ge(x_first_loaded[0], LOAD)
            for n in range(CT):
                transpose_x(x_first, 0, n)
            pe.wait_ge(silu_ready, 1)
            pe.wait_ge(w2_t_ready, 1)
            gate_layer(z2_ps, w2_t, silu2).then_inc(z2_product, 1)
            for n in range(CT, HALVES * CT):
                transpose_x(x_first, 0, n)
            pe.wait_ge(ones_ready, 1)
            pe.wait_ge(b_split_ready, 3)
            lay_bias(0, 0)
            lay_bias(0, 1)
            pe.wait_ge(wh_loaded, DMA)
            for k in range(HALVES):
                for m in range(HALVES):
                    recur(0, k, m, wh_sb, q_t[:, k, :])
            pe.wait_ge(wx_loaded, DMA)
            for k in range(HALVES):
                pe.wait_ge(x1_t_ready, k + 1)
                for m in range(HALVES):
                    done = lay_input(0, k, 0, m, 0)
            done.then_inc(pre_ready, 1)

            def first_fill(r):
                if r == 0:
                    for n in (2, 3):
                        lay_bias(0, n)
                    for k in range(HALVES):
                        for m in range(HALVES):
                            lay_input(0, k, 1, m, 0)
                if r in (1, 2, 3, 4):
                    pe.wait_ge(x1_t_ready, 2 * HALVES)
                    e, k = (r + 1) % 2, (r - 1) // 2
                    for m in range(HALVES):
                        lay_input(0, k, e, m, 1, whole=(r == 4 and m == HALVES - 1))
                if r == 0:
                    pe.wait_ge(g_tile_ready, 1)
                    for k in range(HALVES):
                        done = nc.tensor.transpose(g_rows_ps[:, k * P:(k + 1) * P],
                                                   g_t_tile[:, k, :, :].rearrange("p s b -> p (s b)"), identity[:])
                    done.then_inc(g_transposed, 1)
                if r in (1, 2):
                    pe.wait_ge(x_first_loaded[1], LOAD)
                    for n in range((r - 1) * CT, r * CT):
                        transpose_x(x_first, 1, n)
                if r in (3, 4):
                    lay_bias(1, 2 * (r - 3))
                    lay_bias(1, 2 * (r - 3) + 1)
                if r >= 4:
                    if r == 4:
                        pe.wait_ge(x1_t_ready, 2 * HALVES + 2)
                    if r == 10:
                        pe.wait_ge(x1_t_ready, 2 * HALVES + 4)
                    for n in range((r - 4) * 16 // 12, (r - 3) * 16 // 12):
                        lay_nth(1, n)
                if r >= 2 * TS:
                    if r == 2 * TS:
                        pe.wait_ge(x_loaded[0], LOAD)
                        pe.wait_ge(x1_t_ready, 2 * HALVES + 4)
                    transpose_x(x_raw, 0, r - 2 * TS)

            def fill(i, s, first, last):
                c, slot, r = 2 * i + s // CS, s // CS, s % CS
                group, phase = r // TS, r % TS
                if first and slot == 0:
                    first_fill(r)
                elif not (last and slot == 1):
                    if r == 0:
                        pe.wait_ge(x1_t_ready, 2 * HALVES * (c + 1) + 2)
                    if r == 2 * CT:
                        pe.wait_ge(x1_t_ready, 2 * HALVES * (c + 1) + 4)
                    if r in (0, 2, 4, 6):
                        lay_bias(1 - slot, r // 2)
                    lay_nth(1 - slot, r)
                if phase in (0, TS - 1) and not last and not (first and slot == 0):
                    if r == 0:
                        pe.wait_ge(x_loaded[slot], LOAD * (i + 1))
                    transpose_x(x_raw, slot, 2 * group + phase // (TS - 1))
                if phase in (1, 2) and not (first and slot == 0 and group == 0):
                    tile = (CT * slot + group - 1) % PT
                    if phase == 1 and not (first and CT * slot + group - 1 < 2):
                        pe.wait_ge(out_ready, CT * c + group - 2)
                    transpose_h(tile, phase - 1)

            def turn(i, first=False, last=False):
                for s in range(PS):
                    t = PS * i + s
                    if not (first and s == 0):
                        pe.wait_ge(h1_ready, t)
                        if first and s == 1:
                            pe.wait_ge(wh_cast, 3)
                        for k in range(HALVES):
                            for m in range(HALVES):
                                for weights in (wh_a, wh_b, wh_c):
                                    recur(s, k, m, weights, h1[:, (s - 1) % 2, k, :])
                        for k in range(HALVES):
                            pe.wait_ge(h2_ready[k], t)
                            for m in range(HALVES):
                                recur(s, k, m, wh_a, h2[:, (s - 1) % 2, k, :])
                                done = recur(s, k, m, wh_b, h2[:, (s - 1) % 2, k, :], stop=(k == HALVES - 1))
                        done.then_inc(pre_ready, 1)
                    fill(i, s, first, last)

            turn(0, first=True)
            with pe.Fori(1, PAIRS - 1) as i:
                turn(i)
            turn(PAIRS - 1, last=True)
            for m in range(HALVES):
                pe.wait_ge(h_ready[m], T)
            pe.wait_ge(out_ready, T // TS - 2)
            for m in range(HALVES):
                transpose_h(PT - 1, m)

        @block.vector
        def _(dve):
            def scale_rows(place, c, slot, tile):
                return nc.vector.tensor_tensor(x1_rows[:, bass.ds(CT * c + tile, 1), :].rearrange("p a d -> p (a d)"),
                                               place[:, slot, tile, :], g_rows[:], ALU.mult)

            def scale_transposed(c, slot, k, part):
                dve.wait_ge(x_transposed, HALVES * c + k + 1)
                cols = slice(part * CS // 2 * B, (part + 1) * CS // 2 * B)
                nc.vector.tensor_tensor(x1_t[:, k, slot, cols].rearrange("p (s b) -> p s b", b=B),
                                        x_t_ps[k][:, cols].rearrange("p (s b) -> p s b", b=B),
                                        g_t[:, k, :].unsqueeze(1).to_broadcast([P, CS // 2, B]), ALU.mult)\
                    .then_inc(x1_t_ready, 1)

            def add_rows(j, slot, tile):
                dve.wait_ge(h_rows_ready, j + 1)
                nc.vector.tensor_tensor(out_rows[:, slot, tile, :], h_rows_ps[tile % 2][:, 0:D],
                                        x1_rows[:, bass.ds(j, 1), :].rearrange("p a d -> p (a d)"), ALU.add)\
                    .then_inc(out_ready, 1)

            dve.wait_ge(q_transposed, 1)
            nc.vector.tensor_copy(q_t[:].rearrange("p k b -> p (k b)"), q_t_ps).then_inc(q_ready, 1)
            dve.wait_ge(w1_transposed, 1)
            nc.vector.tensor_copy(w1_t[:].rearrange("p k n -> p (k n)"), w1_t_ps).then_inc(w1_t_ready, 1)
            dve.wait_ge(w2_transposed, 1)
            nc.vector.tensor_copy(w2_t[:].rearrange("p k n -> p (k n)"), w2_t_ps).then_inc(w2_t_ready, 1)
            dve.wait_ge(gate_bias_transposed, 1)
            nc.vector.tensor_copy(gate_bias[:], gate_bias_ps[:, 0:2 * HALVES]).then_inc(gate_bias_ready, 1)
            dve.wait_ge(gate_bias_ready, 1)
            for layer, (z_product, z_ps, half) in enumerate(((z1_product, z1_ps, 1.0), (z2_product, z2_ps, 0.5))):
                dve.wait_ge(z_product, 1)
                for m in range(HALVES):
                    done = nc.vector.tensor_scalar(z[:, m, :], z_ps[:, m * B:(m + 1) * B], half,
                                                   gate_bias[:, layer * HALVES + m:layer * HALVES + m + 1],
                                                   ALU.mult, ALU.add)
                done.then_inc(z_ready, 1)
                dve.wait_ge(tanh_z_ready, layer + 1)
                if layer == 0:
                    nc.vector.scalar_tensor_tensor(out=silu2[:], in0=tanh_z[:], scalar=1.0, in1=z[:],
                                                   op0=ALU.add, op1=ALU.mult).then_inc(silu_ready, 1)
                    dve.wait_ge(wh_cast, 1)
                    nc.vector.tensor_tensor(wh_rest[:], wh_sb[:], wh_a[:], ALU.subtract).then_inc(wh_less, 1)
            nc.vector.tensor_scalar(g_t[:], tanh_z[:], 0.5, 2.5, ALU.mult, ALU.add).then_inc(g_t_ready, 1)
            dve.wait_ge(g_t_ready, 1)
            for part in range(2):
                for k in range(HALVES):
                    scale_transposed(0, 0, k, part)
            dve.wait_ge(wh_cast, 2)
            nc.vector.tensor_tensor(wh_last[:], wh_rest[:], wh_b[:], ALU.subtract).then_inc(wh_less, 1)
            for k in range(HALVES):
                done = nc.vector.tensor_copy(g_t_tile[:, k, :, :], g_t[:, k, :].unsqueeze(1).to_broadcast([P, TS, B]))
            done.then_inc(g_tile_ready, 1)

            def first_between(s):
                if s == 1:
                    dve.wait_ge(g_transposed, 1)
                    nc.vector.tensor_copy(g_rows[:], g_rows_ps).then_inc(g_rows_ready, 1)
                if s in (1, 2):
                    for part in range(2):
                        scale_transposed(1, 1, s - 1, part)
                if s == 3:
                    dve.wait_ge(g_rows_ready, 1)
                if s in (3, 5, 6, 9):
                    done = scale_rows(x_first, 0, 0, (3, 5, 6, 9).index(s))
                    if s == 9:
                        done.then_inc(x1_rows_ready, 1)
                if s in (10, 14, CS + 5, CS + 6):
                    done = scale_rows(x_first, 1, 1, (10, 14, CS + 5, CS + 6).index(s))
                    if s == CS + 6:
                        done.then_inc(x1_rows_ready, 1)

            def between(i, s, first, last):
                c, slot, r = 2 * i + s // CS, s // CS, s % CS
                group, phase = r // TS, r % TS
                early = first and slot == 0
                if phase == (2 if early else 0) and not last:
                    if group == 0:
                        dve.wait_ge(x_loaded[slot], LOAD * (i + 1))
                    if early and group == 0:
                        dve.wait_ge(g_rows_ready, 1)
                    done = scale_rows(x_raw, c + 2, slot, group)
                    if group == CT - 1:
                        done.then_inc(x1_rows_ready, 1)
                if phase in (1, 2) and group == 0 and not (last and slot == 1) and not early:
                    if phase == 1:
                        dve.wait_ge(inputs_laid, c)
                    scale_transposed(c + 1, 1 - slot, 1, phase - 1)
                if phase in (1, 2) and group == (3 if early else 2) and not last:
                    if phase == 1:
                        dve.wait_ge(inputs_laid, c + 1)
                    scale_transposed(c + 2, slot, 0, phase - 1)
                if phase == TS - 1 and not (first and slot == 0 and group == 0):
                    tile, out_slot = (group - 1) % CT, slot if group else 1 - slot
                    if tile == 0 and not first:
                        dve.wait_ge(out_stored[out_slot], LOAD * i)
                    add_rows(CT * c + group - 1, out_slot, tile)

            def turn(i, first=False, last=False):
                for s in range(PS):
                    for m in range(HALVES):
                        dve.wait_ge(h_ready[m], PS * i + s + 1)
                        nc.vector.tensor_tensor(h2[:, s % 2, m, :], h_t[:, m, s, :], h1[:, s % 2, m, :], ALU.subtract)\
                            .then_inc(h2_ready[m], 1)
                    between(i, s, first, last)
                    if first:
                        first_between(s)

            turn(0, first=True)
            with dve.Fori(1, PAIRS - 1) as i:
                turn(i)
            turn(PAIRS - 1, last=True)
            add_rows(T // TS - 1, 1, CT - 1)


_INS = ["x", "cond_1024", "L0_cond_W1", "L0_cond_b1", "L0_cond_W2", "L0_cond_b2", "L1_cond_Wx", "L1_cond_Wh",
        "L1_cond_b"]


def kernel(**inputs):
    import numpy as np
    import concourse.bacc as bacc
    from concourse.bass_utils import run_bass_kernel_spmd

    nc = bacc.Bacc("TRN2", target_bir_lowering=False, num_devices=1)
    arrays, args = {}, []
    for name in _INS:
        a = np.ascontiguousarray(inputs[name])
        arrays[f"in_{name}"] = a
        args.append(nc.dram_tensor(f"in_{name}", a.shape, mybir.dt.from_np(a.dtype), kind="ExternalInput").ap())
    args.append(nc.dram_tensor("out_dram", inputs["x"].shape, F32, kind="ExternalOutput").ap())
    build(nc, *args)
    r = run_bass_kernel_spmd(nc, [arrays], core_ids=[0])
    return r.results[0]["out_dram"]
```

```python
from contextlib import ExitStack

import concourse.bass as bass
from concourse import mybir

F32 = mybir.dt.float32
BF16 = mybir.dt.bfloat16
F16 = mybir.dt.float16
ALU = mybir.AluOpType
ACT = mybir.ActivationFunctionType

P = 128
DMA = 16


def build(nc, x, cond, w1, b1, w2, b2, wx, wh, b, out):
    B, T, D = x.shape
    HALVES = D // P
    TS = P // B
    CT = 512 // P
    CS = CT * TS
    PS = 2 * CS
    PT = 2 * CT
    PAIRS = T // PS
    CHUNKS = T // CS
    LOAD = DMA * CT
    assert (B, D, HALVES) == (32, 256, 2) and T % PS == 0 and PAIRS >= 3

    x_view = x.rearrange("b (c t q) d -> c t q b d", t=CT, q=TS)
    out_view = out.rearrange("b (c t q) d -> c t q b d", t=CT, q=TS)

    with ExitStack() as ctx:
        def sb(name, shape, dt=F32):
            return ctx.enter_context(nc.sbuf_tensor(name, shape, dt))

        def sem(name):
            return ctx.enter_context(nc.semaphore(name))

        w1_sb = sb("w1_sb", [P, HALVES, D])
        w2_sb = sb("w2_sb", [P, HALVES, D])
        wx_sb = sb("wx_sb", [P, HALVES, D])
        wh_sb = sb("wh_sb", [P, HALVES, D])
        cond_sb = sb("cond_sb", [B, D])
        bias_rows = sb("bias_rows", [3 * HALVES, P])
        identity = sb("identity", [P, P])
        ones = sb("ones", [P, 256], BF16)

        wh_a = sb("wh_a", [P, HALVES, D], BF16)
        wh_b = sb("wh_b", [P, HALVES, D], BF16)
        wh_c = sb("wh_c", [P, HALVES, D], BF16)
        wh_rest = sb("wh_rest", [P, HALVES, D])
        wh_last = sb("wh_last", [P, HALVES, D])

        w1_t = sb("w1_t", [P, HALVES, D])
        w2_t = sb("w2_t", [P, HALVES, D])
        q_t = sb("q_t", [P, HALVES, B])
        bias = sb("bias", [P, 3 * HALVES])
        half_b2 = sb("half_b2", [P, HALVES])
        z = sb("z", [P, HALVES, B])
        tanh_z = sb("tanh_z", [P, HALVES, B])
        silu2 = sb("silu2", [P, HALVES, B])
        g_t = sb("g_t", [P, HALVES, B])
        g_t_tile = sb("g_t_tile", [P, HALVES, TS, B])
        g_rows = sb("g_rows", [P, D])

        b_parts = sb("b_parts", [P, HALVES, 3], BF16)
        b_rest = sb("b_rest", [P, HALVES])
        b_parts32 = sb("b_parts32", [P, HALVES, 3])
        b_split = sb("b_split", [3, D], BF16)

        x_first = sb("x_first", [P, 2, CT, D])
        x_raw = sb("x_raw", [P, 2, CT, D])
        x1_rows = sb("x1_rows", [P, T // TS, D])
        x1_t = sb("x1_t", [P, HALVES, 2, CS * B])
        h_t = sb("h_t", [P, HALVES, PS, B])
        h1 = sb("h1", [P, 2, HALVES, B], F16)
        h2 = sb("h2", [P, 2, HALVES, B], F16)
        out_rows = sb("out_rows", [P, 2, CT, D])

        pre = [[ctx.enter_context(nc.psum_tensor(f"pre_{s}{e}", [P, CS // 2, HALVES, B], F32)) for e in range(2)]
               for s in range(2)]
        x_t_ps = [ctx.enter_context(nc.psum_tensor(f"x_t_ps_{k}", [P, CT * P], F32)) for k in range(HALVES)]
        h_rows_ps = [ctx.enter_context(nc.psum_tensor(f"h_rows_ps_{s}", [P, 512], F32)) for s in range(2)]
        w1_t_ps, w2_t_ps = [pre[1][e][:].rearrange("p s m b -> p (s m b)") for e in range(2)]
        z1_ps = h_rows_ps[0][:, 0:HALVES * B]
        z2_ps = h_rows_ps[0][:, HALVES * B:2 * HALVES * B]
        q_t_ps = h_rows_ps[1][:, 0:HALVES * B]
        bias_ps = h_rows_ps[1][:, HALVES * B:HALVES * (B + 3)]
        b_split_ps = pre[0][1][:].rearrange("p s m b -> p (s m b)")[0:3, 0:D]
        g_rows_ps = h_rows_ps[1][:, 0:D]

        cond_loaded = sem("cond_loaded")
        bias_loaded = sem("bias_loaded")
        w1_loaded = sem("w1_loaded")
        w2_loaded = sem("w2_loaded")
        wx_loaded = sem("wx_loaded")
        wh_loaded = sem("wh_loaded")
        identity_zeroed = sem("identity_zeroed")
        identity_ready = sem("identity_ready")
        ones_ready = sem("ones_ready")
        q_transposed = sem("q_transposed")
        q_ready = sem("q_ready")
        bias_transposed = sem("bias_transposed")
        bias_ready = sem("bias_ready")
        w1_transposed = sem("w1_transposed")
        w1_t_ready = sem("w1_t_ready")
        w2_transposed = sem("w2_transposed")
        w2_t_ready = sem("w2_t_ready")
        z1_product = sem("z1_product")
        z2_product = sem("z2_product")
        half_b2_ready = sem("half_b2_ready")
        z_ready = sem("z_ready")
        tanh_z_ready = sem("tanh_z_ready")
        silu_ready = sem("silu_ready")
        g_t_ready = sem("g_t_ready")
        g_tile_ready = sem("g_tile_ready")
        g_transposed = sem("g_transposed")
        g_rows_ready = sem("g_rows_ready")
        b_step = sem("b_step")
        b_parts_ready = sem("b_parts_ready")
        b_split_transposed = sem("b_split_transposed")
        wh_cast = sem("wh_cast")
        wh_less = sem("wh_less")
        b_split_ready = sem("b_split_ready")

        x_first_loaded = [sem(f"x_first_loaded_{c}") for c in range(2)]
        x_loaded = [sem(f"x_loaded_{s}") for s in range(2)]
        x_transposed = sem("x_transposed")
        x1_t_ready = sem("x1_t_ready")
        x1_first_rows_ready = sem("x1_first_rows_ready")
        x1_rows_ready = sem("x1_rows_ready")
        inputs_laid = sem("inputs_laid")
        pre_ready = sem("pre_ready")
        h1_ready = sem("h1_ready")
        h_ready = [sem(f"h_ready_{m}") for m in range(HALVES)]
        h2_ready = [sem(f"h2_ready_{m}") for m in range(HALVES)]
        h_rows_ready = sem("h_rows_ready")
        out_ready = sem("out_ready")
        out_stored = [sem(f"out_stored_{s}") for s in range(2)]
        out_last_stored = sem("out_last_stored")

        block = ctx.enter_context(nc.Block())

        @block.sync
        def _(sp):
            def load(place, c, slot, loaded):
                for tile in range(CT):
                    sp.dma_start(place[:, slot, tile, :], x_view[c, tile]).then_inc(loaded, DMA)

            def store(c, slot):
                for tile in range(CT):
                    sp.dma_start(out_view[c, tile], out_rows[:, slot, tile, :]).then_inc(out_stored[slot], DMA)

            def turn(i, first=False, before_last=False, last=False):
                for s in range(2):
                    c = 2 * i + s
                    if not (first and s == 0) and not (before_last and s == 1) and not last:
                        sp.wait_ge(x_transposed, HALVES * (c + 2))
                        sp.wait_ge(x1_rows_ready, c + 2)
                        load(x_raw, c + 3, 1 - s, x_loaded[1 - s])
                    if not (first and s == 0):
                        sp.wait_ge(out_ready, CT * c)
                        store(c - 1, 1 - s)

            sp.dma_start(cond_sb[:], cond).then_inc(cond_loaded, DMA)
            for n, row in enumerate((b1, b2, b)):
                sp.dma_start(bias_rows[n * HALVES:(n + 1) * HALVES, :], row.rearrange("(k p) -> k p", p=P))\
                    .then_inc(bias_loaded, DMA)
            for c in range(2):
                load(x_first, c, c, x_first_loaded[c])
            for c in range(2):
                load(x_raw, c + 2, c, x_loaded[c])
            turn(0, first=True)
            with sp.Fori(1, PAIRS - 2) as i:
                turn(i)
            turn(PAIRS - 2, before_last=True)
            turn(PAIRS - 1, last=True)
            for tile in range(CT):
                sp.wait_ge(out_ready, CT * (CHUNKS - 1) + tile + 1)
                sp.dma_start(out_view[CHUNKS - 1, tile], out_rows[:, 1, tile, :]).then_inc(out_last_stored, DMA)
            sp.wait_ge(out_stored[0], LOAD * (CHUNKS // 2))
            sp.wait_ge(out_stored[1], LOAD * (CHUNKS // 2 - 1))
            sp.wait_ge(out_last_stored, LOAD)

        @block.gpsimd
        def _(pool):
            nc.gpsimd.memset(identity[:], 0.0).then_inc(identity_zeroed, 1)
            pool.wait_ge(identity_zeroed, 1)
            nc.gpsimd.affine_select(out=identity[:], in_=identity[:], compare_op=ALU.not_equal, fill=1.0, base=0,
                                    pattern=[[-1, P]], channel_multiplier=1).then_inc(identity_ready, 1)
            pool.dma_start(wh_sb[:], wh.rearrange("(k p) n -> p k n", p=P)).then_inc(wh_loaded, DMA)
            b_cols = bias[:, 2 * HALVES:3 * HALVES]
            pool.wait_ge(bias_ready, 1)
            nc.gpsimd.tensor_copy(b_parts[:, :, 0], b_cols).then_inc(b_step, 1)
            pool.wait_ge(b_step, 1)
            nc.gpsimd.tensor_tensor(b_rest[:], b_cols, b_parts[:, :, 0], ALU.subtract).then_inc(b_step, 1)
            pool.wait_ge(b_step, 2)
            nc.gpsimd.tensor_copy(b_parts[:, :, 1], b_rest[:]).then_inc(b_step, 1)
            pool.wait_ge(b_step, 3)
            nc.gpsimd.tensor_tensor(b_parts[:, :, 2], b_rest[:], b_parts[:, :, 1], ALU.subtract).then_inc(b_step, 1)
            pool.wait_ge(b_step, 4)
            nc.gpsimd.tensor_copy(b_parts32[:], b_parts[:]).then_inc(b_parts_ready, 1)
            pool.wait_ge(wh_cast, 2)
            nc.gpsimd.tensor_tensor(wh_last[:], wh_rest[:], wh_b[:], ALU.subtract).then_inc(wh_less, 1)
            pool.wait_ge(g_rows_ready, 1)
            for c in range(2):
                pool.wait_ge(x_first_loaded[c], LOAD)
                for tile in range(CT):
                    nc.gpsimd.tensor_tensor(x1_rows[:, CT * c + tile, :], x_first[:, c, tile, :], g_rows[:], ALU.mult)\
                        .then_inc(x1_first_rows_ready, 1)
            pool.wait_ge(x1_first_rows_ready, 2 * CT)
            pool.sem_inc(x1_rows_ready, 2)

        @block.scalar
        def _(act):
            act.dma_start(w1_sb[:], w1.rearrange("(k p) n -> p k n", p=P)).then_inc(w1_loaded, DMA)
            act.dma_start(w2_sb[:], w2.rearrange("(k p) n -> p k n", p=P)).then_inc(w2_loaded, DMA)
            act.dma_start(wx_sb[:], wx.rearrange("(k p) n -> p k n", p=P)).then_inc(wx_loaded, DMA)
            act.wait_ge(w2_transposed, 1)
            nc.scalar.activation(w2_t[:].rearrange("p k n -> p (k n)"), w2_t_ps, ACT.Copy).then_inc(w2_t_ready, 1)
            act.wait_ge(wh_loaded, DMA)
            nc.scalar.activation(wh_a[:], wh_sb[:], ACT.Copy).then_inc(wh_cast, 1)
            act.wait_ge(z_ready, 1)
            nc.scalar.activation(tanh_z[:], z[:], ACT.Tanh, scale=0.5).then_inc(tanh_z_ready, 1)
            act.wait_ge(wh_less, 1)
            nc.scalar.activation(wh_b[:], wh_rest[:], ACT.Copy).then_inc(wh_cast, 1)
            act.wait_ge(half_b2_ready, 1)
            act.wait_ge(z2_product, 1)
            for m in range(HALVES):
                done = nc.scalar.activation(tanh_z[:, m, :], z2_ps[:, m * B:(m + 1) * B], ACT.Tanh,
                                            bias=half_b2[:, m:m + 1], scale=0.25)
            done.then_inc(tanh_z_ready, 1)
            act.wait_ge(wh_less, 2)
            nc.scalar.activation(wh_c[:], wh_last[:], ACT.Copy).then_inc(wh_cast, 1)

            def step(t, s):
                z_t = pre[s // CS][s % 2][:, s % CS // 2, :, :]
                act.wait_ge(pre_ready, t + 1)
                nc.scalar.activation(h1[:, s % 2, :, :], z_t, ACT.Tanh).then_inc(h1_ready, 1)
                for m in range(HALVES):
                    nc.scalar.activation(h_t[:, m, s, :], z_t[:, m, :], ACT.Tanh).then_inc(h_ready[m], 1)

            with act.Fori(0, PAIRS) as i:
                for s in range(PS):
                    step(PS * i + s, s)

        @block.tensor
        def _(pe):
            def transpose_x(place, slot, n):
                k, tile = n // CT, n % CT
                done = nc.tensor.transpose(x_t_ps[k][:, tile * P:(tile + 1) * P],
                                           place[:, slot, tile, k * P:(k + 1) * P], identity[:])
                if tile == CT - 1:
                    done.then_inc(x_transposed, 1)

            def lay_bias(slot, n, opens=True):
                e, m = n // HALVES, n % HALVES
                nc.tensor.matmul(pre[slot][e][:, :, m, :], b_split[:, m * P:(m + 1) * P], ones[0:3, 0:CS // 2 * B],
                                 start=(opens and m == 0), stop=False, skip_group_check=True)

            def lay_input(slot, k, e, m, part, whole=False):
                steps = slice(part * CS // 4, (part + 1) * CS // 4)
                x1_steps = x1_t[:, k, slot, :].rearrange("p (s e b) -> p s e b", e=2, b=B)[:, steps, e, :]
                done = nc.tensor.matmul(pre[slot][e][:, steps, m, :], wx_sb[:, k, m * P:(m + 1) * P], x1_steps,
                                        start=False, stop=False, skip_group_check=True)
                if whole:
                    done.then_inc(inputs_laid, 1)
                return done

            def lay_nth(slot, n):
                lay_input(slot, n // 8, n // 4 % 2, n // 2 % 2, n % 2, whole=(n == 15))

            def recur(s, k, m, weights, h_part, start=False, stop=False):
                return nc.tensor.matmul(pre[s // CS][s % 2][:, s % CS // 2, m, :], weights[:, k, m * P:(m + 1) * P],
                                        h_part, start=start, stop=stop, skip_group_check=True)

            def transpose_h(tile, half):
                done = nc.tensor.transpose(h_rows_ps[tile % 2][:, half * P:(half + 1) * P],
                                           h_t[:, half, tile * TS:(tile + 1) * TS, :].rearrange("p s b -> p (s b)"),
                                           identity[:])
                if half == HALVES - 1:
                    done.then_inc(h_rows_ready, 1)

            def transpose_weights(w_t_ps, w_sb):
                for k in range(HALVES):
                    for m in range(HALVES):
                        done = nc.tensor.transpose(w_t_ps[:, k * D + m * P:k * D + (m + 1) * P],
                                                   w_sb[:, m, k * P:(k + 1) * P], identity[:])
                return done

            def gate_layer(z_ps, w_t, operand):
                for m in range(HALVES):
                    for k in range(HALVES):
                        done = nc.tensor.matmul(z_ps[:, m * B:(m + 1) * B], w_t[:, k, m * P:(m + 1) * P],
                                                operand[:, k, :], start=(k == 0), stop=(k == HALVES - 1))
                return done

            def warm_up(n):
                for _ in range(n):
                    nc.tensor.matmul(pre[0][0][:, 0:CS // 4], ones[:, 0:P], ones[:], start=True, stop=True)

            pe.wait_ge(ones_ready, 1)
            warm_up(9)
            pe.wait_ge(identity_ready, 1)
            pe.wait_ge(cond_loaded, DMA)
            for k in range(HALVES):
                done = nc.tensor.transpose(q_t_ps[:, k * B:(k + 1) * B], cond_sb[:, k * P:(k + 1) * P],
                                           identity[0:B, 0:B])
            done.then_inc(q_transposed, 1)
            warm_up(6)
            pe.wait_ge(w1_loaded, DMA)
            transpose_weights(w1_t_ps, w1_sb).then_inc(w1_transposed, 1)
            pe.wait_ge(w2_loaded, DMA)
            transpose_weights(w2_t_ps, w2_sb).then_inc(w2_transposed, 1)
            pe.wait_ge(bias_loaded, 3 * DMA)
            pe.wait_ge(q_ready, 1)
            nc.tensor.transpose(bias_ps, bias_rows[:], identity[0:3 * HALVES, 0:3 * HALVES])\
                .then_inc(bias_transposed, 1)
            pe.wait_ge(w1_t_ready, 1)
            gate_layer(z1_ps, w1_t, q_t).then_inc(z1_product, 1)
            pe.wait_ge(wh_loaded, DMA)
            for k in range(HALVES):
                for m in range(HALVES):
                    recur(0, k, m, wh_sb, q_t[:, k, :], start=(k == m == 0))
            pe.wait_ge(b_parts_ready, 1)
            for m in range(HALVES):
                done = nc.tensor.transpose(b_split_ps[:, m * P:(m + 1) * P], b_parts32[:, m, :], identity[:])
            done.then_inc(b_split_transposed, 1)
            pe.wait_ge(silu_ready, 1)
            pe.wait_ge(w2_t_ready, 1)
            gate_layer(z2_ps, w2_t, silu2).then_inc(z2_product, 1)
            pe.wait_ge(x_first_loaded[0], LOAD)
            for n in range(HALVES * CT):
                transpose_x(x_first, 0, n)
            pe.wait_ge(b_split_ready, 1)
            lay_bias(0, 0, opens=False)
            lay_bias(0, 1)
            pe.wait_ge(wx_loaded, DMA)
            for k in range(HALVES):
                pe.wait_ge(x1_t_ready, k + 1)
                for m in range(HALVES):
                    done = lay_input(0, k, 0, m, 0)
            done.then_inc(pre_ready, 1)

            def first_fill(r):
                if r == 0:
                    for n in (2, 3):
                        lay_bias(0, n)
                    for k in range(HALVES):
                        for m in range(HALVES):
                            lay_input(0, k, 1, m, 0)
                if 1 <= r <= 2 * CT:
                    if r == 1:
                        pe.wait_ge(x1_t_ready, 2 * HALVES)
                    n = (r - 1) // 2
                    lay_input(0, n // HALVES, (r + 1) % 2, n % HALVES, 1, whole=(r == 2 * CT))
                if r == 0:
                    pe.wait_ge(g_tile_ready, 1)
                    for k in range(HALVES):
                        done = nc.tensor.transpose(g_rows_ps[:, k * P:(k + 1) * P],
                                                   g_t_tile[:, k, :, :].rearrange("p s b -> p (s b)"), identity[:])
                    done.then_inc(g_transposed, 1)
                if r in (1, 2, 3, 4):
                    if r == 1:
                        pe.wait_ge(x_first_loaded[1], LOAD)
                        pe.wait_ge(x1_t_ready, 2 * HALVES)
                    for n in (2 * (r - 1), 2 * (r - 1) + 1):
                        transpose_x(x_first, 1, n)
                if r in (5, 6):
                    lay_bias(1, 2 * (r - 5))
                    lay_bias(1, 2 * (r - 5) + 1)
                if r >= 7:
                    if r == 7:
                        pe.wait_ge(x1_t_ready, 2 * HALVES + 2)
                    if r == 11:
                        pe.wait_ge(x1_t_ready, 2 * HALVES + 4)
                    for n in range((r - 7) * 16 // 9, (r - 6) * 16 // 9):
                        lay_nth(1, n)
                if r >= 2 * TS:
                    if r == 2 * TS:
                        pe.wait_ge(x_loaded[0], LOAD)
                        pe.wait_ge(x1_t_ready, 2 * HALVES + 4)
                    transpose_x(x_raw, 0, r - 2 * TS)

            def fill(i, s, first, last):
                c, slot, r = 2 * i + s // CS, s // CS, s % CS
                group, phase = r // TS, r % TS
                if first and slot == 0:
                    first_fill(r)
                elif not (last and slot == 1):
                    if r == 0:
                        pe.wait_ge(x1_t_ready, 2 * HALVES * (c + 1) + 2)
                    if r == 2 * CT:
                        pe.wait_ge(x1_t_ready, 2 * HALVES * (c + 1) + 4)
                    if r in (0, 2, 4, 6):
                        lay_bias(1 - slot, r // 2)
                    lay_nth(1 - slot, r)
                if phase in (0, TS - 1) and not last and not (first and slot == 0):
                    if r == 0:
                        pe.wait_ge(x_loaded[slot], LOAD * (i + 1))
                    transpose_x(x_raw, slot, 2 * group + phase // (TS - 1))
                if phase in (1, 2) and not (first and slot == 0 and group == 0):
                    tile = (CT * slot + group - 1) % PT
                    if phase == 1 and not (first and CT * slot + group - 1 < 2):
                        pe.wait_ge(out_ready, CT * c + group - 2)
                    transpose_h(tile, phase - 1)
                if last and slot == 1:
                    warm_up(2)

            def turn(i, first=False, last=False):
                for s in range(PS):
                    t = PS * i + s
                    if not (first and s == 0):
                        pe.wait_ge(h1_ready, t)
                        if first and s == 1:
                            pe.wait_ge(wh_cast, 3)
                        for k in range(HALVES):
                            for m in range(HALVES):
                                for weights in (wh_a, wh_b, wh_c):
                                    recur(s, k, m, weights, h1[:, (s - 1) % 2, k, :])
                        for k in range(HALVES):
                            pe.wait_ge(h2_ready[k], t)
                            for m in range(HALVES):
                                recur(s, k, m, wh_a, h2[:, (s - 1) % 2, k, :])
                                done = recur(s, k, m, wh_b, h2[:, (s - 1) % 2, k, :], stop=(k == HALVES - 1))
                        done.then_inc(pre_ready, 1)
                    fill(i, s, first, last)

            turn(0, first=True)
            with pe.Fori(1, PAIRS - 1) as i:
                turn(i)
            turn(PAIRS - 1, last=True)
            for m in range(HALVES):
                pe.wait_ge(h_ready[m], T)
            pe.wait_ge(out_ready, T // TS - 2)
            for m in range(HALVES):
                transpose_h(PT - 1, m)

        @block.vector
        def _(dve):
            def scale_rows(place, c, slot, tile):
                return nc.vector.tensor_tensor(x1_rows[:, bass.ds(CT * c + tile, 1), :].rearrange("p a d -> p (a d)"),
                                               place[:, slot, tile, :], g_rows[:], ALU.mult)

            def scale_transposed(c, slot, k, part):
                dve.wait_ge(x_transposed, HALVES * c + k + 1)
                cols = slice(part * CS // 2 * B, (part + 1) * CS // 2 * B)
                nc.vector.tensor_tensor(x1_t[:, k, slot, cols].rearrange("p (s b) -> p s b", b=B),
                                        x_t_ps[k][:, cols].rearrange("p (s b) -> p s b", b=B),
                                        g_t[:, k, :].unsqueeze(1).to_broadcast([P, CS // 2, B]), ALU.mult)\
                    .then_inc(x1_t_ready, 1)

            def add_rows(j, slot, tile):
                dve.wait_ge(h_rows_ready, j + 1)
                nc.vector.tensor_tensor(out_rows[:, slot, tile, :], h_rows_ps[tile % 2][:, 0:D],
                                        x1_rows[:, bass.ds(j, 1), :].rearrange("p a d -> p (a d)"), ALU.add)\
                    .then_inc(out_ready, 1)

            nc.vector.memset(ones[:], 1.0).then_inc(ones_ready, 1)
            dve.wait_ge(q_transposed, 1)
            nc.vector.tensor_copy(q_t[:].rearrange("p k b -> p (k b)"), q_t_ps).then_inc(q_ready, 1)
            dve.wait_ge(w1_transposed, 1)
            nc.vector.tensor_copy(w1_t[:].rearrange("p k n -> p (k n)"), w1_t_ps).then_inc(w1_t_ready, 1)
            dve.wait_ge(bias_transposed, 1)
            nc.vector.tensor_copy(bias[:], bias_ps).then_inc(bias_ready, 1)
            dve.wait_ge(bias_ready, 1)
            nc.vector.tensor_scalar(half_b2[:], bias[:, HALVES:2 * HALVES], 0.5, None, ALU.mult)\
                .then_inc(half_b2_ready, 1)
            dve.wait_ge(z1_product, 1)
            for m in range(HALVES):
                done = nc.vector.tensor_scalar(z[:, m, :], z1_ps[:, m * B:(m + 1) * B], bias[:, m:m + 1], None, ALU.add)
            done.then_inc(z_ready, 1)
            dve.wait_ge(tanh_z_ready, 1)
            nc.vector.scalar_tensor_tensor(out=silu2[:], in0=tanh_z[:], scalar=1.0, in1=z[:],
                                           op0=ALU.add, op1=ALU.mult).then_inc(silu_ready, 1)
            dve.wait_ge(wh_cast, 1)
            nc.vector.tensor_tensor(wh_rest[:], wh_sb[:], wh_a[:], ALU.subtract).then_inc(wh_less, 1)
            dve.wait_ge(b_split_transposed, 1)
            nc.vector.tensor_copy(b_split[:], b_split_ps).then_inc(b_split_ready, 1)
            dve.wait_ge(tanh_z_ready, 2)
            nc.vector.tensor_scalar(g_t[:], tanh_z[:], 0.5, 2.5, ALU.mult, ALU.add).then_inc(g_t_ready, 1)
            dve.wait_ge(g_t_ready, 1)
            for part in range(2):
                for k in range(HALVES):
                    scale_transposed(0, 0, k, part)
            for k in range(HALVES):
                done = nc.vector.tensor_copy(g_t_tile[:, k, :, :], g_t[:, k, :].unsqueeze(1).to_broadcast([P, TS, B]))
            done.then_inc(g_tile_ready, 1)

            def first_between(s):
                if s == 1:
                    dve.wait_ge(g_transposed, 1)
                    nc.vector.tensor_copy(g_rows[:], g_rows_ps).then_inc(g_rows_ready, 1)
                if s in (3, 4, 5, 6):
                    scale_transposed(1, 1, (s - 3) // 2, (s - 3) % 2)

            def between(i, s, first, last):
                c, slot, r = 2 * i + s // CS, s // CS, s % CS
                group, phase = r // TS, r % TS
                early = first and slot == 0
                if phase == (2 if early else 0) and not last:
                    if group == 0:
                        dve.wait_ge(x_loaded[slot], LOAD * (i + 1))
                    if early and group == 0:
                        dve.wait_ge(g_rows_ready, 1)
                    done = scale_rows(x_raw, c + 2, slot, group)
                    if group == CT - 1:
                        done.then_inc(x1_rows_ready, 1)
                if phase in (1, 2) and group == 0 and not (last and slot == 1) and not early:
                    if phase == 1:
                        dve.wait_ge(inputs_laid, c)
                    scale_transposed(c + 1, 1 - slot, 1, phase - 1)
                if phase in (1, 2) and group == (3 if early else 2) and not last:
                    if phase == 1:
                        dve.wait_ge(inputs_laid, c + 1)
                    scale_transposed(c + 2, slot, 0, phase - 1)
                if phase == TS - 1 and not (first and slot == 0 and group == 0):
                    tile, out_slot = (group - 1) % CT, slot if group else 1 - slot
                    if tile == 0 and not first:
                        dve.wait_ge(out_stored[out_slot], LOAD * i)
                    if first:
                        tiles = CT * slot + group
                        dve.wait_ge(x1_first_rows_ready, tiles + (tiles == PT - 1))
                    add_rows(CT * c + group - 1, out_slot, tile)

            def turn(i, first=False, last=False):
                for s in range(PS):
                    for m in range(HALVES):
                        dve.wait_ge(h_ready[m], PS * i + s + 1)
                        nc.vector.tensor_tensor(h2[:, s % 2, m, :], h_t[:, m, s, :], h1[:, s % 2, m, :], ALU.subtract)\
                            .then_inc(h2_ready[m], 1)
                    between(i, s, first, last)
                    if first:
                        first_between(s)

            turn(0, first=True)
            with dve.Fori(1, PAIRS - 1) as i:
                turn(i)
            turn(PAIRS - 1, last=True)
            add_rows(T // TS - 1, 1, CT - 1)


_INS = ["x", "cond_1024", "L0_cond_W1", "L0_cond_b1", "L0_cond_W2", "L0_cond_b2", "L1_cond_Wx", "L1_cond_Wh",
        "L1_cond_b"]


def kernel(**inputs):
    import numpy as np
    import concourse.bacc as bacc
    from concourse.bass_utils import run_bass_kernel_spmd

    nc = bacc.Bacc("TRN2", target_bir_lowering=False, num_devices=1)
    arrays, args = {}, []
    for name in _INS:
        a = np.ascontiguousarray(inputs[name])
        arrays[f"in_{name}"] = a
        args.append(nc.dram_tensor(f"in_{name}", a.shape, mybir.dt.from_np(a.dtype), kind="ExternalInput").ap())
    args.append(nc.dram_tensor("out_dram", inputs["x"].shape, F32, kind="ExternalOutput").ap())
    build(nc, *args)
    r = run_bass_kernel_spmd(nc, [arrays], core_ids=[0])
    return r.results[0]["out_dram"]
```
